# Optimizing a Trainium2 kernel written in Bass

```python
import numpy as np
import jax
import jax.numpy as jnp

def _softmax(x, axis=-1):
    return jax.nn.softmax(x, axis=axis)

def _gelu(x):
    return jax.nn.gelu(x, approximate=True)

def _silu(x):
    return jax.nn.silu(x)

def _sigmoid(x):
    return jax.nn.sigmoid(x)

def _layernorm(x, axis=-1, eps=1e-05):
    m = jnp.mean(x, axis=axis, keepdims=True)
    v = jnp.var(x, axis=axis, keepdims=True)
    return (x - m) / jnp.sqrt(v + eps)

def _scatter_add(tgt, idx, src, axis=0):
    return tgt.at[idx].add(src)

def _segment_sum(src, seg, n):
    return jax.ops.segment_sum(src, seg, n)
kernel_name = 'mk_adaln_d1_jaxref_r4_270ce2'

def setup_inputs(seed: int=0):
    np.random.seed(seed)
    _w = jnp.asarray

    def _L0_attn_setup():
        import jax, jax.numpy as jnp
        import numpy as np
        DIM_MODEL = 256
        NUM_HEADS = 16
        B, T = (4, 256)

        def rel_sinusoidal_enc(seq_len, dim_model):
            pos = jnp.concatenate([jnp.arange(seq_len - 1, 0, -1, dtype=jnp.float32), jnp.arange(0, -seq_len, -1, dtype=jnp.float32)])
            inv_freq = 1.0 / 10000.0 ** (2.0 * jnp.arange(dim_model // 2, dtype=jnp.float32) / dim_model)
            angles = pos[:, None] * inv_freq[None, :]
            enc = jnp.stack([jnp.sin(angles), jnp.cos(angles)], axis=-1)
            return enc.reshape(2 * seq_len - 1, dim_model)

        def rel_to_abs(s):
            b, h, l1, l2 = s.shape
            s = jnp.pad(s, ((0, 0), (0, 0), (0, 0), (0, 1)))
            s = s.reshape(b, h, l1 * (l2 + 1))
            s = jnp.pad(s, ((0, 0), (0, 0), (0, l2 - l1)))
            s = s.reshape(b, h, 1 + l1, l2)
            return s[:, :, :l1, l1 - 1:]
        key = jax.random.key(seed)
        ks = jax.random.split(key, 6)
        D = DIM_MODEL
        scale = 1.0 / np.sqrt(D)
        return {'x': jax.random.normal(ks[0], (B, T, D), dtype=jnp.float32), 'Wq': jax.random.normal(ks[1], (D, D), dtype=jnp.float32) * scale, 'bq': jnp.zeros((D,), dtype=jnp.float32), 'Wk': jax.random.normal(ks[2], (D, D), dtype=jnp.float32) * scale, 'bk': jnp.zeros((D,), dtype=jnp.float32), 'Wv': jax.random.normal(ks[3], (D, D), dtype=jnp.float32) * scale, 'bv': jnp.zeros((D,), dtype=jnp.float32), 'Wpos': jax.random.normal(ks[4], (D, D), dtype=jnp.float32) * scale, 'bpos': jnp.zeros((D,), dtype=jnp.float32), 'Wo': jax.random.normal(ks[5], (D, D), dtype=jnp.float32) * scale, 'bo': jnp.zeros((D,), dtype=jnp.float32)}
    _L0_attn_in = _L0_attn_setup()

    def _L0_ffn_setup():
        import jax, jax.numpy as jnp
        import numpy as np
        IN_F, OUT_F, BLOCK, NBLK = (256, 1024, 64, 16)
        TOPK = NBLK // 4
        key = jax.random.key(seed)
        ks = jax.random.split(key, 7)
        s = 1.0 / np.sqrt(IN_F)
        s2 = 1.0 / np.sqrt(OUT_F)
        return {'x': jax.random.normal(ks[0], (4, 1024, IN_F), jnp.float32), 'router_w': jax.random.uniform(ks[1], (NBLK, IN_F), jnp.float32, -s, s), 'router_b': jax.random.uniform(ks[2], (NBLK,), jnp.float32, -s, s), 'w1': jax.random.uniform(ks[3], (OUT_F, IN_F), jnp.float32, -s, s), 'b1': jax.random.uniform(ks[4], (OUT_F,), jnp.float32, -s, s), 'w2': jax.random.uniform(ks[5], (IN_F, OUT_F), jnp.float32, -s2, s2), 'b2': jax.random.uniform(ks[6], (IN_F,), jnp.float32, -s2, s2)}
    _L0_ffn_in = _L0_ffn_setup()
    _L0_c = _w((lambda *s: np.random.randn(*s).astype(np.float32) * 0.05)(16, 256))
    _L0_wmod = _w((lambda *s: np.random.randn(*s).astype(np.float32) * 0.05)(256, 6 * 256) * 256 ** (-0.5))
    _d = {'L0_attn_x': _L0_attn_in['x'], 'L0_attn_Wq': _L0_attn_in['Wq'], 'L0_attn_bq': _L0_attn_in['bq'], 'L0_attn_Wk': _L0_attn_in['Wk'], 'L0_attn_bk': _L0_attn_in['bk'], 'L0_attn_Wv': _L0_attn_in['Wv'], 'L0_attn_bv': _L0_attn_in['bv'], 'L0_attn_Wpos': _L0_attn_in['Wpos'], 'L0_attn_bpos': _L0_attn_in['bpos'], 'L0_attn_Wo': _L0_attn_in['Wo'], 'L0_attn_bo': _L0_attn_in['bo'], 'L0_ffn_router_w': _L0_ffn_in['router_w'], 'L0_ffn_router_b': _L0_ffn_in['router_b'], 'L0_ffn_w1': _L0_ffn_in['w1'], 'L0_ffn_b1': _L0_ffn_in['b1'], 'L0_ffn_w2': _L0_ffn_in['w2'], 'L0_ffn_b2': _L0_ffn_in['b2'], 'L0_c': _L0_c, 'L0_wmod': _L0_wmod}
    _x0 = _d['L0_attn_x']
    _d['L0_attn_x'] = jax.random.normal(jax.random.fold_in(jax.random.key(seed), 1), (16, 512, 256), dtype=_x0.dtype)
    del _x0
    return _d

def reference(L0_attn_x, L0_attn_Wq, L0_attn_bq, L0_attn_Wk, L0_attn_bk, L0_attn_Wv, L0_attn_bv, L0_attn_Wpos, L0_attn_bpos, L0_attn_Wo, L0_attn_bo, L0_ffn_router_w, L0_ffn_router_b, L0_ffn_w1, L0_ffn_b1, L0_ffn_w2, L0_ffn_b2, L0_c, L0_wmod):

    def _L0_attn_ref(x, Wq, bq, Wk, bk, Wv, bv, Wpos, bpos, Wo, bo):
        import jax, jax.numpy as jnp
        import numpy as np
        DIM_MODEL = 256
        NUM_HEADS = 16
        B, T = (4, 256)

        def rel_sinusoidal_enc(seq_len, dim_model):
            pos = jnp.concatenate([jnp.arange(seq_len - 1, 0, -1, dtype=jnp.float32), jnp.arange(0, -seq_len, -1, dtype=jnp.float32)])
            inv_freq = 1.0 / 10000.0 ** (2.0 * jnp.arange(dim_model // 2, dtype=jnp.float32) / dim_model)
            angles = pos[:, None] * inv_freq[None, :]
            enc = jnp.stack([jnp.sin(angles), jnp.cos(angles)], axis=-1)
            return enc.reshape(2 * seq_len - 1, dim_model)

        def rel_to_abs(s):
            b, h, l1, l2 = s.shape
            s = jnp.pad(s, ((0, 0), (0, 0), (0, 0), (0, 1)))
            s = s.reshape(b, h, l1 * (l2 + 1))
            s = jnp.pad(s, ((0, 0), (0, 0), (0, l2 - l1)))
            s = s.reshape(b, h, 1 + l1, l2)
            return s[:, :, :l1, l1 - 1:]
        Bsz, Tlen, D = x.shape
        H = NUM_HEADS
        dh = D // H
        Q = (x @ Wq + bq).reshape(Bsz, Tlen, H, dh).transpose(0, 2, 1, 3)
        K = (x @ Wk + bk).reshape(Bsz, Tlen, H, dh).transpose(0, 2, 1, 3)
        V = (x @ Wv + bv).reshape(Bsz, Tlen, H, dh).transpose(0, 2, 1, 3)
        Epos = rel_sinusoidal_enc(Tlen, D) @ Wpos + bpos
        E = Epos.reshape(2 * Tlen - 1, H, dh)
        scores_K = jnp.einsum('bhqd,bhkd->bhqk', Q, K)
        scores_E = rel_to_abs(jnp.einsum('bhqd,rhd->bhqr', Q, E))
        att = jax.nn.softmax((scores_K + scores_E) / np.sqrt(dh), axis=-1)
        O = jnp.einsum('bhqk,bhkd->bhqd', att, V)
        O = O.transpose(0, 2, 1, 3).reshape(Bsz, Tlen, D)
        return O @ Wo + bo

    def _L0_ffn_ref(x, router_w, router_b, w1, b1, w2, b2):
        import jax, jax.numpy as jnp
        import numpy as np
        IN_F, OUT_F, BLOCK, NBLK = (256, 1024, 64, 16)
        TOPK = NBLK // 4
        x_shape = x.shape
        xf = x.reshape(-1, IN_F)
        n = xf.shape[0]
        prob = jax.nn.softmax(xf @ router_w.T + router_b, axis=-1)
        _, idx = jax.lax.top_k(prob, TOPK)
        mask = jnp.zeros((n, NBLK), bool).at[jnp.arange(n)[:, None], idx].set(True)
        w1b = w1.reshape(NBLK, BLOCK, IN_F)
        b1b = b1.reshape(NBLK, BLOCK)
        h = jnp.einsum('nd,ibd->nib', xf, w1b) + b1b
        h = jnp.where(mask[:, :, None], h, jnp.zeros((), h.dtype))
        h = jax.nn.relu(h)
        w2b = w2.reshape(IN_F, NBLK, BLOCK)
        y = jnp.einsum('nib,dib->nd', jnp.where(mask[:, :, None], h, 0.0), w2b) + b2
        return y.reshape(x_shape)
    x = L0_attn_x
    mod = (_silu(L0_c) @ L0_wmod).reshape(L0_c.shape[0], 6, 1, -1)
    sa, ca, ga, sb, cb, gb = (mod[:, 0], mod[:, 1], mod[:, 2], mod[:, 3], mod[:, 4], mod[:, 5])
    ga = (2 * (ga >= 0) - 1) * jnp.maximum(jnp.abs(ga), 0.25)
    gb = (2 * (gb >= 0) - 1) * jnp.maximum(jnp.abs(gb), 0.25)
    h = _layernorm(x, axis=-1) * (1 + ca) + sa
    x = x + ga * _L0_attn_ref(h, L0_attn_Wq, L0_attn_bq, L0_attn_Wk, L0_attn_bk, L0_attn_Wv, L0_attn_bv, L0_attn_Wpos, L0_attn_bpos, L0_attn_Wo, L0_attn_bo)
    h = _layernorm(x, axis=-1) * (1 + cb) + sb
    x = x + gb * _L0_ffn_ref(h, L0_ffn_router_w, L0_ffn_router_b, L0_ffn_w1, L0_ffn_b1, L0_ffn_w2, L0_ffn_b2)
    return x

_drawn_inputs = setup_inputs


def setup_inputs(seed=0):
    import zlib

    import numpy as np

    out = dict(_drawn_inputs(seed))
    spreads = {'L0_attn_bq': (0.0, 0.8),
     'L0_attn_bk': (0.0, 2.0),
     'L0_attn_bv': (0.0, 0.311),
     'L0_attn_bpos': (0.0, 2.0),
     'L0_attn_bo': (0.0, 0.324)}
    factors = {'L0_attn_Wpos': 4.97, 'L0_ffn_router_b': 23.069, 'L0_ffn_b1': 33.615, 'L0_ffn_b2': 8.0}
    for name, (base, spread) in spreads.items():
        noise = np.random.default_rng([zlib.crc32(name.encode()), seed]).standard_normal(out[name].shape)
        drawn = base * np.exp(spread * noise) if base else spread * noise
        out[name] = jnp.asarray(drawn.astype(out[name].dtype))
    for name, factor in factors.items():
        out[name] = (out[name] * factor).astype(out[name].dtype)
    return out
```

```python
import numpy as np
import concourse.bass as bass
from concourse import mybir

f32 = mybir.dt.float32
f16 = mybir.dt.float16
bf16 = mybir.dt.bfloat16
ALU = mybir.AluOpType
ACT = mybir.ActivationFunctionType
AX = mybir.AxisListType

P = 128
B, T, D, H = 16, 512, 256, 16
DH = D // H
F = 1024
NBLK, TOPK = 16, 4
KD = D // P
NT = T // P
FT = F // P
R, S = 8, 64
G, BG = 4, 4
EW = T + S - 1
RW = 2 * T
WS = 16.0
W2S = 64.0
SOFT = 1.0 / (WS * WS * DH ** 0.5)
EPS = 1e-5
OFF = float(2 ** 60)
SA, CA, GA, SB, CB, GB = range(6)


def low_part(dve, lo, hi, full, scale):
    return dve.scalar_tensor_tensor(out=lo, in0=full, scalar=scale, in1=hi, op0=ALU.mult, op1=ALU.subtract)


def alone(eng, passage):
    eng.sem_inc(passage, 1)


class Chain:

    def __init__(self, eng, sem, base=0):
        self.eng, self.sem, self.base, self.n = eng, sem, base, 0

    def __call__(self, ins):
        self.n += 1
        ins.then_inc(self.sem, 1)
        self.eng.wait_ge(self.sem, self.base + self.n)
        return ins


def load_positions(sp, scr, dst, h, done):
    for r in range(R):
        at = T - S - S * r
        sp.dma_start(dst[r * DH:(r + 1) * DH, :, 0:EW],
                     scr["e"][:, bass.ds(h, 1), :, at:at + EW].rearrange("l o d y -> (o d) l y")).then_inc(done, 16)


def spread_sums(sp, scr, name, h, sums, store):
    a = scr["o"][bass.ds(h, 1), DH] if name == "o" else scr["inv"][bass.ds(h, 1)]
    a = a.rearrange("o b (c i) -> (o b c) i", i=B * T // P)
    return sp.dma_start(a, sums[:, :]) if store else sp.dma_start(sums[:, :], a)


def project(nc, io, scr, keep, sb, pb, sem):
    v_all, mods, ident = keep["v_all"], keep["mods"], keep["ident"]
    x_in = sb("x_in", [P, 2, NT, D], f32)
    stats = sb("stats", [P, 2, NT, 6], f32)
    mv = sb("mv", [P, 2, NT, 2], f32)
    vare = sb("vare", [P, 2, NT], f32)
    rstd = sb("rstd", [P, 2, NT], f32)
    xn = sb("xn", [P, 2, NT, D], f32)
    h_full = sb("h_full", [P, 2, KD, T], f32)
    h_hi = sb("h_hi", [P, 2, KD, T], f16)
    h_lo = sb("h_lo", [P, 2, KD, T], f16)
    w_full = sb("w_full", [P, KD, 3 * D], f32)
    w_hi = sb("w_hi", [P, KD, 3 * D], f16)
    w_lo = sb("w_lo", [P, KD, 3 * D], f16)
    wpos = sb("wpos", [P, KD, D], f32)
    wpos_hi = sb("wpos_hi", [P, KD, D], f16)
    wpos_lo = sb("wpos_lo", [P, KD, D], f16)
    enc = sb("enc", [P, 2, KD, RW], f16)
    bias = sb("bias", [P, 3, KD], f32)
    qk_hi = sb("qk_hi", [P, 2, 2 * KD, T], f16)
    qk_lo = sb("qk_lo", [P, 2, 2 * KD, T], f16)
    e_hi = sb("e_hi", [P, KD, RW], f16)
    e_lo = sb("e_lo", [P, KD, RW], f16)
    cT = sb("cT", [P, KD, B], f32)
    c_e = sb("c_e", [P, KD, B], f32)
    c_r = sb("c_r", [P, KD, B], f32)
    silu = sb("silu", [P, KD, B], f32)
    wmod = sb("wmod", [P, KD, 6 * D], f32)
    g_row = sb("g_row", [B, 2, D], f32)
    g_sign = sb("g_sign", [B, 2, D], f32)
    bob2 = sb("bob2", [B, 2, D], f32)
    rows = sb("rows", [B, 4, D], f32)
    half = sb("half", [P, NT], f32)

    t_ps = pb("t_ps", [P, KD, T], f32)
    qk_ps = pb("qk_ps", [P, 2 * KD, T], f32)
    v_ps = pb("v_ps", [P, 2, 2, D], f32)

    c_in, small_in = sem("c_in"), sem("small_in1")
    wmod_in = [sem(f"wmod_in{i}") for i in range(3)]
    gates_in = sem("gates_in")
    w_in, pos_in = sem("w_in"), sem("pos_in")
    x_loaded = [sem("x_loaded0"), sem("x_loaded1")]
    dve_own = sem("dve_own")
    half_set = sem("half_set")
    e_neg = sem("e_neg")
    silu_ready = sem("silu_ready")
    gates_out = sem("gates_out")
    mods_ps = sem("mods_ps")
    rows_ready = sem("rows_ready")
    bias_ready = sem("bias_ready")
    whi_ready = sem("whi_ready")
    wlo_ready = sem("wlo_ready")
    poslo_ready = sem("poslo_ready")
    mods_ready = sem("mods_ready")
    stats_ready = sem("stats_ready")
    aggr_ready = sem("aggr_ready")
    vare_ready = sem("vare_ready")
    rstd_ready = sem("rstd_ready")
    xn_ready = sem("xn_ready")
    t_ready = sem("t_ready")
    h_ready = sem("h_ready")
    hi_ready = sem("hi_ready")
    lo_ready = sem("lo_ready")
    qk_ready = sem("qk_ready")
    qkhi_ready = sem("qkhi_ready")
    qklo_ready = sem("qklo_ready")
    v_ready = sem("v_ready")
    v_stored = sem("v_stored")
    e_ready = sem("e_ready")
    ehi_ready = sem("ehi_ready")
    elo_ready = sem("elo_ready")
    out_done = [sem("out_done0"), sem("out_done1")]
    misc_done = sem("misc_done")
    e_stored = sem("e_stored")
    passage = sem("passage")

    NSMALL = 4
    OUTS = 12
    last = B - 1
    x4 = io["x"].rearrange("b (t p) d -> b p t d", p=P)

    def load_x(eng, b, par):
        eng.dma_start(x_in[:, par], x4[bass.ds(b, 1)].rearrange("o p t d -> p (o t) d"))\
            .then_inc(x_loaded[par], 16)

    def store_rows(eng, b, par, hl, m):
        src, hs = (qk_hi, qk_lo)[hl], slice(m * H // KD, (m + 1) * H // KD)
        eng.dma_start(scr["qk"][hl, hs, bass.ds(b, 1)].rearrange("h o d i -> h (o d) i"), src[:, par, m])\
            .then_inc(out_done[par], 16)

    by_scalar = ((0, 2), (0, 3))

    with nc.Block() as block:
        @block.sync
        def _(sp):
            def store_qk(b, par):
                one = bass.ds(b, 1)
                for m in range(2 * KD):
                    sp.wait_ge(qklo_ready, 2 * KD * b + m + 1)
                    for hl, src in enumerate((qk_hi, qk_lo)):
                        if m < KD:
                            sp.dma_start(scr["q_split"][hl, :, m * P:(m + 1) * P, one, :]
                                         .rearrange("r p o s -> p (r o) s"),
                                         src[:, par, m].rearrange("p (r s) -> p r s", r=R)).then_inc(out_done[par], 16)
                        if (hl, m) not in by_scalar:
                            store_rows(sp, b, par, hl, m)

            kp = lambda ap: ap.rearrange("(k p) n -> p k n", p=P)
            sp.dma_start(ident[:, :], io["ident"]).then_inc(small_in, 16)
            load_x(sp, 0, 0)
            for n, w in enumerate(("wq", "wk", "wv")):
                sp.dma_start(w_full[:, :, n * D:(n + 1) * D], kp(io[w])).then_inc(w_in, 16)
            with nc.allow_non_contiguous_dma(reason="biases, 256 elements each"):
                for n, w in enumerate(("bq", "bk", "bpos")):
                    sp.dma_start(bias[:, n], io[w].rearrange("(k p) -> p k", p=P)).then_inc(small_in, 16)
            load_x(sp, 1, 1)
            for n, w in enumerate(("bo", "b2")):
                sp.dma_start(bob2[:, n], io[w].rearrange("(a n) -> a n", a=1).to_broadcast([B, D]))\
                    .then_inc(gates_in, 16)
            sp.dma_start(keep["bv"][:, :], io["bv2"]).then_inc(gates_in, 16)
            sp.wait_ge(xn_ready, 1)
            load_x(sp, 2, 0)
            sp.wait_ge(elo_ready, 2 * KD)
            for hl, part in enumerate((e_hi, e_lo)):
                for k in range(KD):
                    dst = scr["e"][hl, k * H // KD:(k + 1) * H // KD]
                    sp.dma_start(dst.rearrange("h d y -> (h d) y"), part[:, k]).then_inc(e_stored, 16)
            sp.wait_ge(e_stored, 16 * 2 * KD)
            for hp in (0, 1):
                load_positions(sp, scr, keep["e_shift"][hp], hp, keep["e_in"][hp])
            sp.wait_ge(rows_ready, 1)
            sp.dma_start(scr["rows"], rows[:, :, :]).then_inc(misc_done, 16)
            with sp.Fori(0, B // 2) as bb:
                for par in (0, 1):
                    store_qk(bb * 2 + par, par)
            sp.wait_ge(misc_done, 16)
            for par in (0, 1):
                sp.wait_ge(out_done[par], 16 * OUTS * (B // 2 + 1))

        @block.scalar
        def _(act):
            kp = lambda ap: ap.rearrange("(k p) n -> p k n", p=P)
            act.dma_start(cT[:, :, :], kp(io["cT"])).then_inc(c_in, 16)
            for n in range(3):
                cols = slice(2 * n * D, 2 * (n + 1) * D)
                act.dma_start(wmod[:, :, cols], kp(io["wmod"])[:, :, cols]).then_inc(wmod_in[n], 16)
                if n == 0:
                    act.dma_start(wpos[:, :, :], kp(io["wpos"])).then_inc(pos_in, 16)
            act.dma_start(enc[:, :, :, :], io["enc"]).then_inc(pos_in, 16)
            act.wait_ge(c_in, 16)
            nc.scalar.activation(c_e[:, :, :], cT[:, :, :], ACT.Exp, scale=-1.0).then_inc(e_neg, 1)

            def norm_out(b, par):
                act.wait_ge(t_ready, b + 1)
                for k in range(KD):
                    last_ = nc.scalar.activation(h_full[:, par, k], t_ps[:, k], ACT.Identity,
                                                 bias=mods[:, KD * SA + k, bass.ds(b, 1)],
                                                 scale=mods[:, KD * CA + k, bass.ds(b, 1)])
                last_.then_inc(h_ready, 1)

            def qkv_out(i, par):
                b = 2 * i + par
                act.wait_ge(out_done[par], (i + 1) * 16 * OUTS)
                for m in range(2 * KD):
                    act.wait_ge(qk_ready, 2 * KD * b + m + 1)
                    nc.scalar.activation(qk_hi[:, par, m], qk_ps[:, m], ACT.Identity,
                                         bias=bias[:, m // KD, m % KD:m % KD + 1]).then_inc(qkhi_ready, 1)
                for j in range(2):
                    act.wait_ge(v_ready, 2 * b + j + 1)
                    nc.scalar.copy(v_all[:, bass.ds(NT * b + 2 * j, 2), :], v_ps[:, j]).then_inc(v_stored, 1)
                    if j == 0:
                        act.wait_ge(qkhi_ready, 2 * KD * (b + 1))
                        for hl, m in by_scalar:
                            store_rows(act, b, par, hl, m)

            act.wait_ge(pos_in, 32)
            nc.scalar.mul(wpos_hi[:, :, :], wpos[:, :, :], WS).then_inc(whi_ready, 1)
            act.wait_ge(w_in, 48)
            nc.scalar.mul(w_hi[:, :, :], w_full[:, :, :], WS).then_inc(whi_ready, 1)
            act.wait_ge(mods_ready, 1)
            norm_out(0, 0)
            act.wait_ge(bias_ready, 1)
            for par in (0, 1):
                act.sem_inc(out_done[par], 16 * OUTS)
            for n in range(2 * KD):
                act.wait_ge(e_ready, n + 1)
                nc.scalar.activation(e_hi[:, n // 2, (n % 2) * T:(n % 2) * T + T], qk_ps[:, n], ACT.Identity,
                                     bias=bias[:, 2, n // 2:n // 2 + 1]).then_inc(ehi_ready, 1)

            def load_ahead(b, par):
                act.wait_ge(xn_ready, b + 2)
                load_x(act, b + 3, 1 - par)

            with act.Fori(0, B // 2 - 2) as bb:
                for par in (0, 1):
                    norm_out(bb * 2 + par + 1, 1 - par)
                    load_ahead(bb * 2 + par, par)
                    qkv_out(bb, par)
            norm_out(B - 3, 1)
            load_ahead(B - 4, 0)
            qkv_out(B // 2 - 2, 0)
            norm_out(B - 2, 0)
            qkv_out(B // 2 - 2, 1)
            norm_out(last, 1)
            qkv_out(B // 2 - 1, 0)
            qkv_out(B // 2 - 1, 1)

        @block.gpsimd
        def _(pool):
            nc.gpsimd.memset(half[:, :], -0.5).then_inc(half_set, 1)
            pool.wait_ge(half_set, 1)

            def rsqrt(b, par):
                pool.wait_ge(vare_ready, b + 1)
                nc.gpsimd.tensor_tensor(rstd[:, par], vare[:, par], half[:, :], ALU.pow).then_inc(rstd_ready, 1)

            def low(b, par):
                pool.wait_ge(hi_ready, b + 1)
                nc.gpsimd.tensor_tensor(h_lo[:, par], h_full[:, par], h_hi[:, par], ALU.subtract)\
                    .then_inc(lo_ready, 1)

            with pool.Fori(0, B // 2) as bb:
                for par in (0, 1):
                    rsqrt(bb * 2 + par, par)
                    low(bb * 2 + par, par)

        @block.vector
        def _(dve):
            own = Chain(dve, dve_own)

            def norm(i, par):
                b = 2 * i + par
                dve.wait_ge(x_loaded[par], 16 * i + 16)
                for t in range(NT):
                    nc.vector.bn_stats(stats[:, par, t], x_in[:, par, t]).then_inc(stats_ready, 1)
                dve.wait_ge(stats_ready, NT * (b + 1))
                alone(dve, passage)
                for t in range(NT):
                    nc.vector.bn_aggr(mv[:, par, t], stats[:, par, t]).then_inc(aggr_ready, 1)
                dve.wait_ge(aggr_ready, NT * (b + 1))
                nc.vector.tensor_scalar(vare[:, par], mv[:, par, :, 1], EPS, None, ALU.add).then_inc(vare_ready, 1)
                dve.wait_ge(rstd_ready, b + 1)
                for t in range(NT):
                    last_ = nc.vector.tensor_scalar(xn[:, par, t], x_in[:, par, t], mv[:, par, t, 0:1],
                                                    rstd[:, par, t:t + 1], ALU.subtract, ALU.mult)
                last_.then_inc(xn_ready, 1)

            def high(b, par):
                dve.wait_ge(h_ready, b + 1)
                nc.vector.tensor_copy(h_hi[:, par], h_full[:, par]).then_inc(hi_ready, 1)

            def qk_low(b, par):
                for m in range(2 * KD):
                    dve.wait_ge(qkhi_ready, 2 * KD * b + m + 1)
                    nc.vector.scalar_tensor_tensor(out=qk_lo[:, par, m], in0=qk_ps[:, m],
                                                   scalar=bias[:, m // KD, m % KD:m % KD + 1],
                                                   in1=qk_hi[:, par, m], op0=ALU.add, op1=ALU.subtract)\
                        .then_inc(qklo_ready, 1)

            dve.wait_ge(e_neg, 1)
            own(nc.vector.tensor_scalar(c_r[:, :, :], c_e[:, :, :], 1.0, None, ALU.add))
            own(nc.vector.reciprocal(c_e[:, :, :], c_r[:, :, :]))
            nc.vector.tensor_tensor(silu[:, :, :], cT[:, :, :], c_e[:, :, :], ALU.mult).then_inc(silu_ready, 1)
            norm(0, 0)
            dve.wait_ge(small_in, 16 * NSMALL)
            nc.vector.tensor_scalar(bias[:, :, :], bias[:, :, :], WS, None, ALU.mult).then_inc(bias_ready, 1)
            dve.wait_ge(bias_ready, 1)
            first = qk_ps[:, 3, 0:2 * KD * B].rearrange("p (m b) -> p m b", b=B)
            dve.wait_ge(mods_ps, 1)
            own(nc.vector.tensor_copy(mods[:, KD * SA:KD * SA + KD], first[:, KD * SA:KD * SA + KD]))
            nc.vector.tensor_scalar(mods[:, KD * CA:KD * CA + KD], first[:, KD * CA:KD * CA + KD],
                                    1.0, None, ALU.add).then_inc(mods_ready, 1)
            dve.wait_ge(whi_ready, 1)
            low_part(nc.vector, wpos_lo[:, :, :], wpos_hi[:, :, :], wpos[:, :, :], WS).then_inc(poslo_ready, 1)
            dve.wait_ge(whi_ready, 2)
            low_part(nc.vector, w_lo[:, :, :], w_hi[:, :, :], w_full[:, :, :], WS).then_inc(wlo_ready, 1)
            high(0, 0)
            norm(0, 1)
            dve.wait_ge(mods_ps, 2)
            own(nc.vector.tensor_copy(mods[:, KD * GA:], v_ps[:, 1].rearrange("p a n -> p (a n)")[:, 0:4 * KD * B]
                                      .rearrange("p (m b) -> p m b", b=B)))
            nc.vector.tensor_copy(g_row[:, :, :], v_ps[0:B, 0]).then_inc(gates_out, 1)
            for n in range(2 * KD):
                dve.wait_ge(ehi_ready, n + 1)
                nc.vector.scalar_tensor_tensor(out=e_lo[:, n // 2, (n % 2) * T:(n % 2) * T + T], in0=qk_ps[:, n],
                                               scalar=bias[:, 2, n // 2:n // 2 + 1],
                                               in1=e_hi[:, n // 2, (n % 2) * T:(n % 2) * T + T],
                                               op0=ALU.add, op1=ALU.subtract).then_inc(elo_ready, 1)

            own(nc.vector.tensor_scalar(mods[:, KD * CB:KD * CB + KD], mods[:, KD * CB:KD * CB + KD],
                                        1.0, None, ALU.add))
            dve.wait_ge(gates_in, 48)
            own(nc.vector.tensor_scalar(g_sign[:, :, :], g_row[:, :, :], 0.0, 2.0, ALU.is_ge, ALU.mult))
            own(nc.vector.tensor_scalar(g_sign[:, :, :], g_sign[:, :, :], -1.0, None, ALU.add))
            own(nc.vector.tensor_tensor(g_row[:, :, :], g_row[:, :, :], g_sign[:, :, :], ALU.mult))
            own(nc.vector.tensor_scalar(g_row[:, :, :], g_row[:, :, :], 0.25, None, ALU.max))
            own(nc.vector.tensor_tensor(g_row[:, :, :], g_row[:, :, :], g_sign[:, :, :], ALU.mult))
            own(nc.vector.tensor_scalar(rows[:, 1], g_row[:, 0], 1.0 / WS, None, ALU.mult))
            own(nc.vector.tensor_tensor(rows[:, 0], g_row[:, 0], bob2[:, 0], ALU.mult))
            own(nc.vector.tensor_scalar(rows[:, 2], g_row[:, 1], 1.0 / W2S, None, ALU.mult))
            nc.vector.tensor_tensor(rows[:, 3], g_row[:, 1], bob2[:, 1], ALU.mult).then_inc(rows_ready, 1)
            with dve.Fori(0, B // 2 - 1) as bb:
                for par in (0, 1):
                    b = bb * 2 + par
                    high(b + 1, 1 - par)
                    norm(bb + 1, par)
                    qk_low(b, par)
            high(last, 1)
            qk_low(B - 2, 0)
            qk_low(last, 1)

        @block.tensor
        def _(pe):
            def turn(b, par):
                pe.wait_ge(xn_ready, b + 1)
                for k in range(KD):
                    for t in range(NT):
                        last_ = nc.tensor.transpose(t_ps[:, k, t * P:(t + 1) * P],
                                                    xn[:, par, t, k * P:(k + 1) * P], ident[:, :])
                last_.then_inc(t_ready, 1)

            def qkv(b, par, first=False):
                pe.wait_ge(lo_ready, b + 1)
                parts = [(hi, w) for hi, w in ((h_hi, w_hi), (h_lo, w_hi), (h_hi, w_lo))]
                for m in range(2 * KD):
                    if first:
                        pe.wait_ge(elo_ready, m + 1)
                    else:
                        pe.wait_ge(qklo_ready, 2 * KD * b + m - 2 * KD + 1)
                    n = 0
                    for k in range(KD):
                        for h, w in parts:
                            last_ = nc.tensor.matmul(qk_ps[:, m], w[:, k, m * P:(m + 1) * P], h[:, par, k],
                                                     start=(n == 0), stop=(n == 3 * KD - 1))
                            n += 1
                    last_.then_inc(qk_ready, 1)
                for t in range(NT):
                    if t % 2 == 0 and not first:
                        pe.wait_ge(v_stored, 2 * b + t // 2 - 1)
                    n = 0
                    for k in range(KD):
                        for h, w in parts:
                            last_ = nc.tensor.matmul(v_ps[:, t // 2, t % 2], h[:, par, k, t * P:(t + 1) * P],
                                                     w[:, k, 2 * D:3 * D], start=(n == 0), stop=(n == 3 * KD - 1))
                            n += 1
                    if t % 2:
                        last_.then_inc(v_ready, 1)

            def modulations(ps, ms):
                for i, m in enumerate(ms):
                    for k in range(KD):
                        last_ = nc.tensor.matmul(ps[:, i * B:(i + 1) * B], wmod[:, k, m * P:(m + 1) * P],
                                                 silu[:, k], start=(k == 0), stop=(k == KD - 1))
                return last_

            pe.wait_ge(silu_ready, 1)
            pe.wait_ge(wmod_in[0], 16)
            modulations(qk_ps[:, 3], range(0, 2 * KD)).then_inc(mods_ps, 1)
            pe.wait_ge(small_in, 16 * NSMALL)
            turn(0, 0)
            pe.wait_ge(wmod_in[1], 16)
            pe.wait_ge(wmod_in[2], 16)
            modulations(v_ps[:, 1].rearrange("p a n -> p (a n)"), range(2 * KD, 6 * KD))
            for n, g in enumerate((GA, GB)):
                for k in range(KD):
                    last_ = nc.tensor.matmul(v_ps[0:B, 0, n], silu[:, k], wmod[:, k, g * D:(g + 1) * D],
                                             start=(k == 0), stop=(k == KD - 1))
            last_.then_inc(mods_ps, 1)
            pe.wait_ge(pos_in, 32)
            pe.wait_ge(poslo_ready, 1)
            for n in range(2 * KD):
                if n == 3:
                    pe.wait_ge(mods_ready, 1)
                i = 0
                for k in range(KD):
                    for w, e in ((wpos_hi, 0), (wpos_lo, 0), (wpos_hi, 1)):
                        last_ = nc.tensor.matmul(qk_ps[:, n], w[:, k, (n // 2) * P:(n // 2 + 1) * P],
                                                 enc[:, e, k, (n % 2) * T:(n % 2) * T + T],
                                                 start=(i == 0), stop=(i == 3 * KD - 1))
                        i += 1
                last_.then_inc(e_ready, 1)
            pe.wait_ge(wlo_ready, 1)
            pe.wait_ge(h_ready, 1)
            turn(1, 1)
            pe.wait_ge(gates_out, 1)
            qkv(0, 0, first=True)
            pe.wait_ge(h_ready, 2)
            turn(2, 0)
            qkv(1, 1)
            with pe.Fori(1, B // 2 - 1) as bb:
                for par in (0, 1):
                    b = bb * 2 + par
                    pe.wait_ge(h_ready, b + 1)
                    turn(b + 1, 1 - par)
                    qkv(b, par)
            pe.wait_ge(h_ready, B - 1)
            turn(last, 1)
            qkv(B - 2, 0)
            qkv(last, 1)


def attend(nc, io, scr, keep, sb, pb, sem):
    v_all, ident = keep["v_all"], keep["ident"]
    NS = 4
    CH = 16
    NCH = S // CH
    q_rep = [sb(f"q_rep{i}", [P, G, T], f16) for i in (0, 1)]
    q_shift = [sb(f"q_shift{i}", [P, 2, B, S], f16) for i in (0, 1)]
    k_rep = [sb(f"k_rep{i}", [P, 2, G, T], f16) for i in (0, 1)]
    e_shift, e_in = keep["e_shift"], keep["e_in"]
    mask_b = sb("mask_b", [P, BG, R], f16)
    mask_r = sb("mask_r", [P, R], f16)
    stat_k = sb("stat_k", [P, NS, G, BG, R], f16)
    stat_e = sb("stat_e", [P, NS, 2, B, R], f16)
    neg_max = sb("neg_max", [P, NS], f32)
    shift = sb("shift", [P, NS], f32)
    probs = sb("probs", [P, NS, T], f32)
    probs_t = [sb(f"probs_t{i}", [P, NT, B * R, CH], f32) for i in (0, 1)]
    v_head = sb("v_head", [P, B * NT, 2 * DH], f32)
    o_acc = sb("o_acc", [P, G, R, S], f32)
    head_sums = sb("head_sums", [P, B * T // P], f32)

    s_ps = pb("s_ps", [P, NS, T], f32)
    t_ps = pb("t_ps2", [P, 2, T], f32)
    o_ps = pb("o_ps", [P, G, P], f32)

    masks_in = sem("masks_in")
    head_in = [sem("head_in0"), sem("head_in1")]
    stat_ready = sem("stat_ready")
    s_ready = sem("s_ready")
    neg_ready = sem("neg_ready")
    shift_ready = sem("shift_ready")
    exp_done = sem("exp_done")
    t_ready = [sem("t_ready0"), sem("t_ready1")]
    t_out = [sem("t_out0"), sem("t_out1")]
    v_ready = sem("v_ready2")
    pv_done = sem("pv_done")
    o_ready = sem("o_ready")
    o_stored = sem("o_stored")
    sums_in, inv_ready, inv_stored = sem("sums_in"), sem("inv_ready"), sem("inv_stored")
    passage_pe, passage_pool, passage_sp = sem("passage_pe"), sem("passage_pool"), sem("passage_sp")

    LOADS = 8
    HC = CH // 2
    LAST = H * NCH
    SET = 3

    with nc.Block() as block:
        @block.sync
        def _(sp):
            sp.dma_start(mask_b[:, :, :], io["mask_b"]).then_inc(masks_in, 16)
            sp.dma_start(mask_r[:, :], io["mask_r"]).then_inc(masks_in, 16)

            def load_head(h, hp):
                rows = bass.ds(h * DH, DH)

                def inc(dst, src):
                    sp.dma_start(dst, src).then_inc(head_in[hp], 16)

                one = bass.ds(h, 1)
                half = BG * DH
                for hl in (0, 1):
                    inc(q_shift[hp][:, hl],
                        scr["q_split"][hl, :, rows, :, :].rearrange("r d b s -> r d (b s)"))
                    inc(q_rep[hp][half * hl:half * hl + half],
                        scr["qk"][hl, one].rearrange("o (g b) d i -> (o b d) g i", g=G))
                    for twice in (0, 1):
                        inc(k_rep[hp][half * twice:half * twice + half, hl],
                            scr["qk"][hl, bass.ds(h + H, 1)].rearrange("o (g b) d i -> (o b d) g i", g=G))

            def store_out(h):
                for g in range(G):
                    dst = scr["o"][bass.ds(h, 1), :, g * BG:(g + 1) * BG, :].rearrange("o m b i -> b (o m) i")
                    sp.dma_start(dst, o_acc[:, g]).then_inc(o_stored, 16)

            def load_sums(h):
                sp.wait_ge(o_stored, 16 * G * (h + 1))
                alone(sp, passage_sp)
                spread_sums(sp, scr, "o", h, head_sums, False).then_inc(sums_in, 16)

            def store_inv(h):
                sp.wait_ge(inv_ready, h + 1)
                alone(sp, passage_sp)
                spread_sums(sp, scr, "inv", h, head_sums, True).then_inc(inv_stored, 16)

            sp.sem_inc(inv_stored, 16)
            load_head(0, 0)
            load_head(1, 1)
            with sp.Fori(0, H // 2 - 1) as hh:
                for hp in (0, 1):
                    h = 2 * hh + hp
                    sp.wait_ge(o_ready, NCH * h + 2)
                    store_out(h)
                    sp.wait_ge(inv_stored, 16 * h + 16)
                    alone(sp, passage_sp)
                    load_sums(h)
                    sp.wait_ge(s_ready, S * (h + 1) + NS)
                    load_head(h + 2, hp)
                    load_positions(sp, scr, e_shift[hp], h + 2, e_in[hp])
                    store_inv(h)
            for h in (H - 2, H - 1):
                sp.wait_ge(o_ready, NCH * h + 2)
                store_out(h)
                sp.wait_ge(inv_stored, 16 * h + 16)
                load_sums(h)
                store_inv(h)
            sp.wait_ge(o_ready, NCH * H + 2)
            store_out(H)
            sp.wait_ge(inv_stored, 16 * H + 16)
            sp.wait_ge(o_stored, 16 * G * (H + 1))

        @block.gpsimd
        def _(pool):
            nc.gpsimd.memset(probs_t[1][:, :, :, :], 1.0).then_inc(v_ready, 1)
            nc.gpsimd.memset(o_acc[:, :, :, :], 1.0).then_inc(v_ready, 1)
            pool.sem_inc(s_ready, NS)
            pool.wait_ge(masks_in, 32)

            def stage(hh, hp, step, n, u):
                pool.wait_ge(s_ready, n + 1)
                q = q_rep[hp].rearrange("p g (r s) -> p g r s", r=R)[:, :, :, bass.ds(step, 1)]
                q = q.rearrange("p g r s -> p g (r s)").unsqueeze(2).to_broadcast([P, G, BG, R])
                m = mask_b[:, :, :].unsqueeze(1).to_broadcast([P, G, BG, R])
                nc.gpsimd.tensor_tensor(stat_k[:, u], q, m, ALU.mult).then_inc(stat_ready, 1)
                q = q_shift[hp][:, :, :, bass.ds(step, 1)].rearrange("p l b s -> p (l b) s")
                m = mask_r[:, :].unsqueeze(1).to_broadcast([P, 2 * B, R])
                nc.gpsimd.tensor_tensor(stat_e[:, u].rearrange("p l b r -> p (l b) r"),
                                        q.to_broadcast([P, 2 * B, R]), m, ALU.mult).then_inc(stat_ready, 1)

            with pool.Fori(0, H // 2) as hh:
                for hp in (0, 1):
                    pool.wait_ge(head_in[hp], 16 * LOADS * (hh + 1))
                    alone(pool, passage_pool)
                    with pool.Fori(0, S // NS) as k:
                        for u in range(NS):
                            stage(hh, hp, NS * k + u, hh * (2 * S) + (S * hp + u) + k * NS, u)

        @block.scalar
        def _(act):
            act.sem_inc(exp_done, NS)
            act.sem_inc(t_out[0], HC)
            act.sem_inc(o_ready, 1)

            def exp(n, u):
                act.wait_ge(shift_ready, n + 1)
                nc.scalar.activation(probs[:, u], s_ps[:, u], ACT.Exp, bias=shift[:, u:u + 1], scale=SOFT)\
                    .then_inc(exp_done, 1)

            def out_even(m, cp, q):
                act.wait_ge(t_ready[0], m + 1)
                nc.scalar.copy(probs_t[cp][:, :, :, bass.ds(q, 1)].rearrange("p j c q -> p j (c q)"),
                               t_ps[:, 0].rearrange("p (j c) -> p j c", j=NT)).then_inc(t_out[0], 1)

            def out_pv(step, at):
                act.wait_ge(pv_done, step + 1)
                nc.scalar.copy(o_acc[:, :, :, bass.ds(at, CH)],
                               o_ps[:, :, :].rearrange("p g (r s) -> p g r s", r=R)).then_inc(o_ready, 1)

            with act.Fori(0, H // 2) as hh:
                for hp in (0, 1):
                    with act.Fori(0, NCH // 2) as cc:
                        for cp in (0, 1):
                            chunk = hh * (2 * NCH) + (NCH * hp + cp) + cc * 2
                            with act.Fori(0, CH // NS) as k:
                                n = chunk * CH + k * NS
                                m = chunk * HC + k * 2
                                exp(n, 0)
                                exp(n + 1, 1)
                                out_even(m, cp, NS * k)
                                exp(n + 2, 2)
                                exp(n + 3, 3)
                                out_even(m + 1, cp, NS * k + 2)
                            if cp:
                                act.wait_ge(o_stored, 16 * G * (hh * 2 + hp + 1))
                                out_pv(chunk, cc * (2 * CH))
                            else:
                                out_pv(chunk, (NCH - 1) * CH - cc * (2 * CH))
            act.wait_ge(o_stored, 16 * G * H)
            out_pv(LAST, (NCH - 1) * CH)

        @block.vector
        def _(dve):
            dve.sem_inc(t_out[1], HC)
            nc.vector.memset(v_head[:, :, :], WS).then_inc(v_ready, 1)

            def row_max(n, u):
                dve.wait_ge(s_ready, n + (NS + 1))
                nc.vector.tensor_reduce(neg_max[:, u:u + 1], s_ps[:, u], AX.X, ALU.max, negate=True)\
                    .then_inc(neg_ready, 1)
                dve.wait_ge(neg_ready, n + 1)
                nc.vector.tensor_scalar(shift[:, u:u + 1], neg_max[:, u:u + 1], SOFT, None, ALU.mult)\
                    .then_inc(shift_ready, 1)

            def out_odd(m, cp, q):
                dve.wait_ge(t_ready[1], m + 1)
                nc.vector.tensor_copy(probs_t[cp][:, :, :, bass.ds(q, 1)].rearrange("p j c q -> p j (c q)"),
                                      t_ps[:, 1].rearrange("p (j c) -> p j c", j=NT)).then_inc(t_out[1], 1)

            with dve.Fori(0, H // 2) as hh:
                for hp in (0, 1):
                    with dve.Fori(0, NCH // 2) as cc:
                        for cp in (0, 1):
                            chunk = hh * (2 * NCH) + (NCH * hp + cp) + cc * 2
                            if cp:
                                dve.wait_ge(pv_done, chunk)
                                nc.vector.tensor_copy(v_head[:, :, 0:DH],
                                                      v_all[:, :, bass.ds((hh * 2 + hp) * DH, DH)])\
                                    .then_inc(v_ready, 1)
                            n, m = chunk * CH, chunk * HC
                            for u in range(NS):
                                row_max(n + u, u)
                            out_odd(m, cp, 1)
                            with dve.Fori(1, CH // NS) as k:
                                n, m = chunk * CH + k * NS, chunk * HC + k * 2
                                row_max(n, 0)
                                out_odd(m - 1, cp, NS * k - 1)
                                for u in range(1, NS):
                                    row_max(n + u, u)
                                out_odd(m, cp, NS * k + 1)
                            out_odd(chunk * HC + (HC - 1), cp, CH - 1)
                    dve.wait_ge(sums_in, 16 * (hh * 2 + hp + 1))
                    nc.vector.reciprocal(head_sums[:, :], head_sums[:, :]).then_inc(inv_ready, 1)

        @block.tensor
        def _(pe):
            def scores(hp, n, at, u):
                pe.wait_ge(exp_done, n + 1)
                pe.wait_ge(stat_ready, n * 2 + 2)
                for i, (ql, el) in enumerate(((0, 0), (1, 0), (0, 1))):
                    nc.tensor.matmul(s_ps[:, u], stat_e[:, u, ql], e_shift[hp][:, el, bass.ds(at, T)],
                                     start=(i == 0), stop=False, skip_group_check=True)
                for kl in (0, 1):
                    for g in range(G):
                        last_ = nc.tensor.matmul(s_ps[32 * g:32 * g + 32, u], stat_k[:, u, g], k_rep[hp][:, kl, g],
                                                 start=False, stop=(kl == 1), skip_group_check=True)
                last_.then_inc(s_ready, 1)

            def turn(n, m, u):
                par = u % 2
                pe.wait_ge(exp_done, n + (NS + 1))
                pe.wait_ge(t_out[par], m + HC)
                for j in range(NT):
                    last_ = nc.tensor.transpose(t_ps[:, par, j * P:(j + 1) * P], probs[:, u, j * P:(j + 1) * P],
                                                ident[:, :])
                last_.then_inc(t_ready[par], 1)

            def values(step, buf, copies):
                for par in (0, 1):
                    pe.wait_ge(t_out[par], step * HC + HC)
                pe.wait_ge(v_ready, copies)
                pe.wait_ge(o_ready, step + 1)
                for g in range(G):
                    for j in range(NT):
                        for b in range(BG):
                            bb = g * BG + b
                            last_ = nc.tensor.matmul(o_ps[32 * b:32 * b + 32, g], v_head[:, bb * NT + j],
                                                     probs_t[buf][:, j, bb * R:(bb + 1) * R, :],
                                                     start=(j == 0), stop=(j == NT - 1), skip_group_check=True)
                last_.then_inc(pv_done, 1)

            with pe.Fori(0, H // 2) as hh:
                for hp in (0, 1):
                    pe.wait_ge(head_in[hp], 16 * LOADS * (hh + 1))
                    pe.wait_ge(e_in[hp], 16 * R * (hh + 1))
                    alone(pe, passage_pe)
                    with pe.Fori(0, NCH // 2) as cc:
                        for cp in (0, 1):
                            chunk = hh * (2 * NCH) + (NCH * hp + cp) + cc * 2
                            at = cc * (-2 * CH) + (S - 1 - CH * cp)

                            def steps(k):
                                n, m = chunk * CH + k * NS, chunk * HC + k * 2
                                scores(hp, n, at + k * -NS, 0)
                                if k > 0:
                                    turn(n - 1, m - 1, 3)
                                scores(hp, n + 1, at + k * -NS - 1, 1)
                                scores(hp, n + 2, at + k * -NS - 2, 2)
                                turn(n, m, 0)
                                scores(hp, n + 3, at + k * -NS - 3, 3)
                                turn(n + 1, m, 1)
                                turn(n + 2, m + 1, 2)

                            for k in range(CH // NS):
                                steps(k)
                            values(chunk, 1 - cp, hh * NCH + (hp * (NCH // 2) + SET + cp) + cc)
                            turn(chunk * CH + (CH - 1), chunk * HC + (HC - 1), 3)
            values(LAST, 1, LAST // 2 + SET)


def ffn(nc, io, scr, keep, sb, pb, sem, out):
    mods, ident, bv = keep["mods"], keep["ident"], keep["bv"]
    NR = 8
    wo_full = sb("wo_full", [P, KD, D], f32)
    w1_full = sb("w1_full", [P, KD, F], f32)
    w2_full = sb("w2_full", [P, FT, D], f32)
    wo_hi, wo_lo = sb("wo_hi", [P, KD, D], f16), sb("wo_lo", [P, KD, D], f16)
    w1_hi, w1_lo = sb("w1_hi", [P, KD, F], f16), sb("w1_lo", [P, KD, F], f16)
    w2_hi, w2_lo = sb("w2_hi", [P, FT, D], f16), sb("w2_lo", [P, FT, D], f16)
    wr_full = sb("wr_full", [P, KD, NBLK], f32)
    wr_hi, wr_lo = sb("wr_hi", [P, KD, NBLK], f16), sb("wr_lo", [P, KD, NBLK], f16)
    b1 = sb("b1", [P, FT], f32)
    rb = sb("rb", [P, NBLK], f32)
    ident_b = sb("ident_b", [P, P], bf16)
    spread = sb("spread", [NBLK, F], bf16)
    half = sb("half3", [P, NT], f32)
    sums = sb("sums", [P, B * T // P], f32)
    x_in = sb("x_in3", [P, 2, NT, D], f32)
    pv = sb("pv", [P, 2, KD, T], f32)
    inv = sb("inv", [P, 2, KD, T], f32)
    ga_bo = sb("ga_bo", [P, 2, D], f32)
    gates = sb("gates", [P, 2, 3, D], f32)
    o_hi, o_lo = sb("o_hi", [P, KD, T], f16), sb("o_lo", [P, KD, T], f16)
    x_bo = sb("x_bo", [P, NT, D], f32)
    x2 = sb("x2", [P, NT, D], f32)
    x2_b2 = sb("x2_b2", [P, 2, NT, D], f32)
    xn = sb("xn3", [P, NT, D], f32)
    stats = sb("stats3", [P, NT, 6], f32)
    mv = sb("mv3", [P, NT, 2], f32)
    vare = sb("vare3", [P, NT], f32)
    rstd = sb("rstd3", [P, NT], f32)
    h_full = sb("h_full3", [P, KD, T], f32)
    h_hi, h_lo = sb("h_hi3", [P, KD, T], f16), sb("h_lo3", [P, KD, T], f16)
    lg = sb("lg", [P, 3, NT, NBLK], f32)
    red = sb("red", [P, 4, NT], f32)
    top8 = sb("top8", [P, NT, 8], f32)
    above = sb("above", [P, NT, NBLK], f32)
    ties = sb("ties", [P, NT, 2 * NBLK], f32)
    run_a = sb("run_a", [P, NT, 2 * NBLK], f32)
    run_b = sb("run_b", [P, NT, 2 * NBLK], f32)
    keep_m = sb("keep_m", [P, NT, NBLK], f32)
    off = sb("off", [P, NT, NBLK], bf16)
    off_t = sb("off_t", [NBLK, T], bf16)
    r_full = sb("r_full", [P, NR, T], f32)
    r_hi, r_lo = sb("r_hi", [P, FT, T], f16), sb("r_lo", [P, FT, T], f16)
    y = sb("y", [P, 2, NT, D], f32)

    a_ps = pb("a_ps", [P, 2 * T], f32)
    l_ps = pb("l_ps", [P, NT, NBLK], f32)
    m_ps = pb("m_ps", [NBLK, T], bf16)
    r_ps = pb("r_ps", [P, 2, T], f32)
    f_ps = pb("f_ps", [P, NT, D], f32)

    names = ("sums_in", "sums_out", "inv_ready", "w_in0", "w_in1", "w_in2", "small_in", "w_split", "whi_ready", "own",
             "half_set", "pv_scaled", "ohi_ready", "olo_ready", "xbo_ready", "wo_ready", "stats_ready", "aggr_ready",
             "max_ready", "vare_ready", "rstd_ready", "xb2_ready", "xn_ready", "t_ready", "h_ready", "hi_ready", "lo_ready",
             "lg_ready", "le_in", "le_out", "off_ready", "offt_ps", "offt_ready", "r_ready", "relu_ready",
             "f_ready", "y_ready", "zeros_set", "passage", "scaled")
    s = {n: sem("f_" + n) for n in names}
    b_in = [sem("f_b_in0"), sem("f_b_in1")]
    g_in = [sem("f_g_in0"), sem("f_g_in1")]
    y_out = [sem("f_y_out0"), sem("f_y_out1")]
    rlo_ready = [sem("f_rlo_ready0"), sem("f_rlo_ready1")]
    NB_IN = 6
    NOWN = 17
    last = B - 1

    with nc.Block() as block:
        @block.sync
        def _(sp):
            x4 = io["x"].rearrange("b (t p) d -> b p t d", p=P)
            out4 = out.rearrange("b (t p) d -> b p t d", p=P)

            def halves(k):
                return slice(1 + k * H // KD, 1 + (k + 1) * H // KD)

            def load_inv(b, par):
                for k in range(KD):
                    sp.dma_start(inv[:, par, k], scr["inv"][halves(k), bass.ds(b, 1), :]
                                 .to_broadcast([H // KD, DH, T])).then_inc(b_in[par], 16)

            def load(b, par):
                def inc(dst, src):
                    sp.dma_start(dst, src).then_inc(b_in[par], 16)

                one = bass.ds(b, 1)
                for k in range(KD):
                    inc(pv[:, par, k], scr["o"][halves(k), 0:DH, one, :].rearrange("h d o i -> h d (o i)"))
                inc(x_in[:, par], x4[one].rearrange("o p t d -> p (o t) d"))
                inc(ga_bo[:, par], scr["rows"][one, 0, :].to_broadcast([P, D]))

            def load_gates(b, par):
                sp.dma_start(gates[:, par], scr["rows"][bass.ds(b, 1), 1:4, :].to_broadcast([P, 3, D]))\
                    .then_inc(g_in[par], 16)

            def load_ahead(b, par):
                sp.wait_ge(s["olo_ready"], b + 1)
                sp.wait_ge(s["xbo_ready"], b + 1)
                load(b + 2, par)
                load_inv(b + 2, par)

            def store(b, par):
                sp.wait_ge(s["y_ready"], b + 1)
                sp.dma_start(out4[bass.ds(b, 1)].rearrange("o p t d -> p (o t) d"), y[:, par])\
                    .then_inc(y_out[par], 16)

            spread_sums(sp, scr, "o", H, sums, False).then_inc(s["sums_in"], 16)
            load(0, 0)
            sp.wait_ge(s["inv_ready"], 1)
            spread_sums(sp, scr, "inv", H, sums, True).then_inc(s["sums_out"], 16)
            sp.wait_ge(s["sums_out"], 16)
            load_inv(0, 0)
            load_gates(0, 0)
            load(1, 1)
            load_inv(1, 1)
            load_gates(1, 1)
            with sp.Fori(0, B // 2 - 1) as bb:
                for par in (0, 1):
                    load_ahead(bb * 2 + par, par)
                    store(bb * 2 + par, par)
                    load_gates(bb * 2 + par + 2, par)
            for par in (0, 1):
                store(B - 2 + par, par)
            for par in (0, 1):
                sp.wait_ge(y_out[par], 16 * (B // 2) + 16)

        @block.scalar
        def _(act):
            kp = lambda ap: ap.rearrange("(k p) n -> p k n", p=P)
            act.dma_start(wo_full[:, :, :], kp(io["wo"])).then_inc(s["w_in0"], 16)
            act.dma_start(wr_full[:, :, :], kp(io["rwT"])).then_inc(s["w_in0"], 16)
            for dst, src in ((b1[:, :], io["b1_2"]), (rb[:, :], io["rb"].rearrange("(a n) -> a n", a=1)
                                                      .to_broadcast([P, NBLK])),
                             (ident_b[:, :], io["ident_b"]), (spread[:, :], io["spread"])):
                act.dma_start(dst, src).then_inc(s["small_in"], 16)
            act.sem_inc(y_out[0], 16)
            act.sem_inc(y_out[1], 16)
            act.wait_ge(s["small_in"], 64)

            def high_weight(hi, full, scale):
                nc.scalar.mul(hi[:, :, :], full[:, :, :], scale).then_inc(s["whi_ready"], 1)

            def o_high(b, par):
                act.wait_ge(s["pv_scaled"], b + 1)
                for k in range(KD):
                    last_ = nc.scalar.activation(o_hi[:, k], pv[:, par, k], ACT.Identity, bias=bv[:, k:k + 1])
                last_.then_inc(s["ohi_ready"], 1)

            def norm_out(b):
                act.wait_ge(s["t_ready"], b + 1)
                for k in range(KD):
                    last_ = nc.scalar.activation(h_full[:, k], a_ps[:, k * T:(k + 1) * T], ACT.Identity,
                                                 bias=mods[:, KD * SB + k, bass.ds(b, 1)],
                                                 scale=mods[:, KD * CB + k, bass.ds(b, 1)])
                last_.then_inc(s["h_ready"], 1)

            def router_exp(b):
                act.wait_ge(s["le_in"], b + 1)
                nc.scalar.activation(lg[:, 1], lg[:, 0], ACT.Exp).then_inc(s["le_out"], 1)

            def router_mask(b):
                act.wait_ge(s["offt_ps"], b + 1)
                nc.scalar.copy(off_t[:, :], m_ps[:, :]).then_inc(s["offt_ready"], 1)

            def relus(b, ms):
                for m in ms:
                    act.wait_ge(s["r_ready"], b * FT + m + 1)
                    act.wait_ge(rlo_ready[m % 2], (b + 1) * (FT // 2))
                    nc.scalar.activation(r_full[:, m % NR], r_ps[:, m % 2], ACT.Relu, bias=b1[:, m:m + 1],
                                         scale=1.0 / WS).then_inc(s["relu_ready"], 1)
                    nc.scalar.activation(r_hi[:, m], r_ps[:, m % 2], ACT.Relu, bias=b1[:, m:m + 1],
                                         scale=1.0 / WS).then_inc(s["relu_ready"], 1)

            def body(b, par, ahead=True):
                relus(b, range(0, FT))
                norm_out(b + 1)
                if ahead:
                    o_high(b + 2, par)
                router_exp(b + 1)
                router_mask(b + 1)

            act.wait_ge(s["w_in0"], 32)
            high_weight(wo_hi, wo_full, WS)
            high_weight(wr_hi, wr_full, WS)
            o_high(0, 0)
            act.dma_start(w1_full[:, :, :], kp(io["w1T"])).then_inc(s["w_in1"], 16)
            act.dma_start(w2_full[:, :, :], kp(io["w2T"])).then_inc(s["w_in2"], 16)
            act.wait_ge(s["w_in1"], 16)
            high_weight(w1_hi, w1_full, WS)
            norm_out(0)
            o_high(1, 1)
            act.wait_ge(s["w_in2"], 16)
            high_weight(w2_hi, w2_full, W2S)
            router_exp(0)
            router_mask(0)
            with act.Fori(0, B // 2 - 1) as bb:
                for par in (0, 1):
                    body(bb * 2 + par, par)
            body(B - 2, 0, ahead=False)
            relus(last, range(0, FT))

        @block.gpsimd
        def _(pool):
            nc.gpsimd.memset(half[:, :], -0.5).then_inc(s["half_set"], 1)
            pool.sem_inc(rlo_ready[0], FT // 2)
            pool.wait_ge(s["half_set"], 1)

            def add_bo(b, par, i):
                pool.wait_ge(b_in[par], 16 * NB_IN * (i + 1))
                nc.gpsimd.tensor_tensor(x_bo[:, :, :], x_in[:, par],
                                        ga_bo[:, par].unsqueeze(1).to_broadcast([P, NT, D]), ALU.add)\
                    .then_inc(s["xbo_ready"], 1)

            def rsqrt(b):
                pool.wait_ge(s["vare_ready"], b + 1)
                nc.gpsimd.tensor_tensor(rstd[:, :], vare[:, :], half[:, :], ALU.pow).then_inc(s["rstd_ready"], 1)

            def add_b2(b, par):
                nc.gpsimd.tensor_tensor(x2_b2[:, par], x2[:, :, :],
                                        gates[:, par, 2].unsqueeze(1).to_broadcast([P, NT, D]), ALU.add)\
                    .then_inc(s["xb2_ready"], 1)

            def relu_low(b, ms):
                for m in ms:
                    pool.wait_ge(s["relu_ready"], b * (2 * FT) + 2 * m + 2)
                    nc.gpsimd.tensor_tensor(r_lo[:, m], r_full[:, m % NR], r_hi[:, m], ALU.subtract)\
                        .then_inc(rlo_ready[0], 1)

            def body(b, par, i, ahead=True):
                relu_low(b, (0, ))
                rsqrt(b + 1)
                relu_low(b, (2, 4, 6))
                add_b2(b + 1, 1 - par)
                if ahead:
                    add_bo(b + 2, par, i + 1)

            add_bo(0, 0, 0)
            rsqrt(0)
            add_b2(0, 0)
            add_bo(1, 1, 0)
            with pool.Fori(0, B // 2 - 1) as bb:
                for par in (0, 1):
                    body(bb * 2 + par, par, bb)
            body(B - 2, 0, 0, ahead=False)
            relu_low(last, (0, 2, 4, 6))

        @block.vector
        def _(dve):
            dve.wait_ge(s["sums_in"], 16)
            nc.vector.reciprocal(sums[:, :], sums[:, :]).then_inc(s["inv_ready"], 1)
            for buf in (ties, run_a, run_b):
                nc.vector.memset(buf[:, :, :], 0.0).then_inc(s["zeros_set"], 1)
            dve.wait_ge(s["zeros_set"], 3)

            def low_weight(n, lo, hi, full, scale):
                dve.wait_ge(s["whi_ready"], n + 1)
                low_part(nc.vector, lo[:, :, :], hi[:, :, :], full[:, :, :], scale).then_inc(s["w_split"], 1)

            def scale_pv(b, par, i):
                dve.wait_ge(b_in[par], 16 * NB_IN * (i + 1))
                nc.vector.tensor_tensor(pv[:, par], pv[:, par], inv[:, par], ALU.mult).then_inc(s["pv_scaled"], 1)
                dve.wait_ge(s["ohi_ready"], b + 1)
                for k in range(KD):
                    last_ = nc.vector.scalar_tensor_tensor(out=o_lo[:, k], in0=pv[:, par, k], scalar=bv[:, k:k + 1],
                                                           in1=o_hi[:, k], op0=ALU.add, op1=ALU.subtract)
                last_.then_inc(s["olo_ready"], 1)

            def residual_norm(b, par, i):
                own = Chain(dve, s["own"], base=b * NOWN)
                dve.wait_ge(g_in[par], 16 * (i + 1))
                dve.wait_ge(s["wo_ready"], b + 1)
                own(nc.vector.tensor_tensor(x2[:, :, :], a_ps[:, :].rearrange("p (t d) -> p t d", t=NT),
                                            gates[:, par, 0].unsqueeze(1).to_broadcast([P, NT, D]), ALU.mult))
                dve.wait_ge(s["xbo_ready"], b + 1)
                own(nc.vector.tensor_tensor(x2[:, :, :], x2[:, :, :], x_bo[:, :, :], ALU.add))
                for t in range(NT):
                    nc.vector.bn_stats(stats[:, t], x2[:, t]).then_inc(s["stats_ready"], 1)
                dve.wait_ge(s["stats_ready"], NT * (b + 1))
                alone(dve, s["passage"])
                for t in range(NT):
                    nc.vector.bn_aggr(mv[:, t], stats[:, t]).then_inc(s["aggr_ready"], 1)
                dve.wait_ge(s["aggr_ready"], NT * (b + 1))
                nc.vector.tensor_scalar(vare[:, :], mv[:, :, 1], EPS, None, ALU.add).then_inc(s["vare_ready"], 1)
                dve.wait_ge(s["rstd_ready"], b + 1)
                for t in range(NT):
                    last_ = nc.vector.tensor_scalar(xn[:, t], x2[:, t], mv[:, t, 0:1], rstd[:, t:t + 1],
                                                    ALU.subtract, ALU.mult)
                last_.then_inc(s["xn_ready"], 1)
                return own

            def high(b):
                dve.wait_ge(s["h_ready"], b + 1)
                nc.vector.tensor_copy(h_hi[:, :, :], h_full[:, :, :]).then_inc(s["hi_ready"], 1)
                dve.wait_ge(s["hi_ready"], b + 1)
                nc.vector.tensor_tensor(h_lo[:, :, :], h_full[:, :, :], h_hi[:, :, :], ALU.subtract)\
                    .then_inc(s["lo_ready"], 1)

            def choose(b, own):
                wide = lambda ap: ap.unsqueeze(2).to_broadcast([P, NT, NBLK])
                z, e, p = lg[:, 0], lg[:, 1], lg[:, 2]
                dve.wait_ge(s["lg_ready"], b + 1)
                own(nc.vector.scalar_tensor_tensor(out=p, in0=l_ps[:, :, :], scalar=1.0 / WS,
                                                   in1=rb[:, :].unsqueeze(1).to_broadcast([P, NT, NBLK]),
                                                   op0=ALU.mult, op1=ALU.add))
                own(nc.vector.tensor_reduce(red[:, 0], p, AX.X, ALU.max))
                nc.vector.tensor_tensor(z, p, wide(red[:, 0]), ALU.subtract).then_inc(s["le_in"], 1)
                dve.wait_ge(s["le_out"], b + 1)
                own(nc.vector.tensor_reduce(red[:, 1], e, AX.X, ALU.add))
                own(nc.vector.reciprocal(red[:, 2], red[:, 1]))
                own(nc.vector.tensor_tensor(p, e, wide(red[:, 2]), ALU.mult))
                alone(dve, s["passage"])
                for t in range(NT):
                    nc.vector.max(top8[:, t], p[:, t]).then_inc(s["max_ready"], 1)
                dve.wait_ge(s["max_ready"], NT * (b + 1))
                least = top8[:, :, TOPK - 1:TOPK].to_broadcast([P, NT, NBLK])
                own(nc.vector.tensor_tensor(above[:, :, :], p, least, ALU.is_gt))
                own(nc.vector.tensor_tensor(ties[:, :, NBLK:], p, least, ALU.is_equal))
                own(nc.vector.tensor_reduce(red[:, 3], above[:, :, :], AX.X, ALU.add))
                src, dst = ties, run_a
                for d in (1, 2, 4, 8):
                    own(nc.vector.tensor_tensor(dst[:, :, NBLK:], src[:, :, NBLK:], src[:, :, NBLK - d:2 * NBLK - d],
                                                ALU.add))
                    src, dst = dst, run_b if dst is run_a else run_a
                own(nc.vector.tensor_tensor(keep_m[:, :, :], src[:, :, NBLK:], wide(red[:, 3]), ALU.add))
                own(nc.vector.scalar_tensor_tensor(out=keep_m[:, :, :], in0=keep_m[:, :, :], scalar=TOPK + 0.5,
                                                   in1=ties[:, :, NBLK:], op0=ALU.is_le, op1=ALU.mult))
                own(nc.vector.tensor_tensor(keep_m[:, :, :], keep_m[:, :, :], above[:, :, :], ALU.add))
                assert own.n == NOWN, own.n
                nc.vector.tensor_scalar(off[:, :, :], keep_m[:, :, :], -1.0, OFF, ALU.add, ALU.mult)\
                    .then_inc(s["off_ready"], 1)

            def relu_low(b, ms):
                for m in ms:
                    dve.wait_ge(s["relu_ready"], b * (2 * FT) + 2 * m + 2)
                    nc.vector.tensor_tensor(r_lo[:, m], r_full[:, m % NR], r_hi[:, m], ALU.subtract)\
                        .then_inc(rlo_ready[1], 1)

            def finish(b, par, i):
                dve.wait_ge(y_out[par], 16 * (i + 1))
                dve.wait_ge(s["f_ready"], b + 1)
                nc.vector.tensor_tensor(y[:, par], f_ps[:, :, :],
                                        gates[:, par, 1].unsqueeze(1).to_broadcast([P, NT, D]), ALU.mult)\
                    .then_inc(s["scaled"], 1)
                dve.wait_ge(s["scaled"], b + 1)
                dve.wait_ge(s["xb2_ready"], b + 1)
                nc.vector.tensor_tensor(y[:, par], y[:, par], x2_b2[:, par], ALU.add).then_inc(s["y_ready"], 1)

            def body(b, par, i, i_next, ahead=True):
                dve.wait_ge(s["xb2_ready"], b + 1)
                own = residual_norm(b + 1, 1 - par, i_next)
                relu_low(b, (1, 3, 5, 7))
                high(b + 1)
                if ahead:
                    scale_pv(b + 2, par, i + 1)
                choose(b + 1, own)
                finish(b, par, i)

            dve.sem_inc(rlo_ready[1], FT // 2)
            low_weight(0, wo_lo, wo_hi, wo_full, WS)
            low_weight(1, wr_lo, wr_hi, wr_full, WS)
            dve.wait_ge(s["small_in"], 64)
            scale_pv(0, 0, 0)
            own0 = residual_norm(0, 0, 0)
            low_weight(2, w1_lo, w1_hi, w1_full, WS)
            high(0)
            scale_pv(1, 1, 0)
            choose(0, own0)
            low_weight(3, w2_lo, w2_hi, w2_full, W2S)
            with dve.Fori(0, B // 2 - 1) as bb:
                for par in (0, 1):
                    body(bb * 2 + par, par, bb, bb + par)
            body(B - 2, 0, B // 2 - 1, B // 2 - 1, ahead=False)
            relu_low(last, (1, 3, 5, 7))
            finish(last, 1, B // 2 - 1)

        @block.tensor
        def _(pe):
            def parts(a_hi, a_lo, b_hi, b_lo):
                return (a_hi, b_hi), (a_lo, b_hi), (a_hi, b_lo)

            def project_out(b):
                pe.wait_ge(s["olo_ready"], b + 1)
                for t in range(NT):
                    n = 0
                    for k in range(KD):
                        for o, w in parts(o_hi, o_lo, wo_hi, wo_lo):
                            last_ = nc.tensor.matmul(a_ps[:, t * D:(t + 1) * D], o[:, k, t * P:(t + 1) * P], w[:, k],
                                                     start=(n == 0), stop=(n == 3 * KD - 1))
                            n += 1
                last_.then_inc(s["wo_ready"], 1)

            def turn(b):
                pe.wait_ge(s["xn_ready"], b + 1)
                for k in range(KD):
                    for t in range(NT):
                        last_ = nc.tensor.transpose(a_ps[:, k * T + t * P:k * T + (t + 1) * P],
                                                    xn[:, t, k * P:(k + 1) * P], ident[:, :])
                last_.then_inc(s["t_ready"], 1)

            def logits(b):
                pe.wait_ge(s["lo_ready"], b + 1)
                for t in range(NT):
                    n = 0
                    for k in range(KD):
                        for h, w in parts(h_hi, h_lo, wr_hi, wr_lo):
                            last_ = nc.tensor.matmul(l_ps[:, t], h[:, k, t * P:(t + 1) * P], w[:, k],
                                                     start=(n == 0), stop=(n == 3 * KD - 1))
                            n += 1
                last_.then_inc(s["lg_ready"], 1)

            def turn_mask(b):
                pe.wait_ge(s["off_ready"], b + 1)
                for t in range(NT):
                    last_ = nc.tensor.transpose(m_ps[:, t * P:(t + 1) * P], off[:, t], ident_b[:, :])
                last_.then_inc(s["offt_ps"], 1)

            def hidden(b, ms, first=False):
                for m in ms:
                    if not (first and m < 2):
                        pe.wait_ge(s["relu_ready"], b * (2 * FT) + 2 * m - 2)
                    cols = slice(m * P, (m + 1) * P)
                    n = 0
                    for k in range(KD):
                        for w, h in ((w1_hi, h_hi), (w1_hi, h_lo), (w1_lo, h_hi)):
                            nc.tensor.matmul(r_ps[:, m % 2], w[:, k, cols], h[:, k], start=(n == 0), stop=False)
                            n += 1
                    if m == 0:
                        pe.wait_ge(s["offt_ready"], b + 1)
                    nc.tensor.matmul(r_ps[:, m % 2], spread[:, cols], off_t[:, :], start=False, stop=True)\
                        .then_inc(s["r_ready"], 1)

            def down(b, ts):
                for t in ts:
                    n = 0
                    for k in range(FT):
                        if t == 0:
                            pe.wait_ge(rlo_ready[k % 2], b * (FT // 2) + (k // 2 + 1 + FT // 2))
                        for r, w in parts(r_hi, r_lo, w2_hi, w2_lo):
                            last_ = nc.tensor.matmul(f_ps[:, t], r[:, k, t * P:(t + 1) * P], w[:, k],
                                                     start=(n == 0), stop=(n == 3 * FT - 1))
                            n += 1
                if NT - 1 in ts:
                    last_.then_inc(s["f_ready"], 1)

            def body(b, first=False):
                if not first:
                    project_out(b + 1)
                turn_mask(b)
                hidden(b, range(0, FT), first)
                turn(b + 1)
                if first:
                    pe.wait_ge(s["w_split"], 4)
                else:
                    pe.wait_ge(s["y_ready"], b)
                down(b, (0, 1))
                logits(b + 1)
                down(b, (2, 3))

            pe.wait_ge(s["w_split"], 2)
            pe.wait_ge(s["small_in"], 64)
            project_out(0)
            turn(0)
            logits(0)
            project_out(1)
            pe.wait_ge(s["w_split"], 3)
            body(0, first=True)
            body(1)
            with nc.Fori(1, B // 2 - 1, engines=[pe.engine], hint_back_edge=True) as bb:
                for par in (0, 1):
                    body(bb * 2 + par)
            body(B - 2)
            turn_mask(last)
            hidden(last, range(0, FT))
            pe.wait_ge(s["y_ready"], last)
            down(last, range(0, NT))


def program(nc, io, out):
    scr = {
        "qk": nc.dram_tensor("qk_scratch", [2, 2 * H, B, DH, T], f16, kind="Internal").ap(),
        "q_split": nc.dram_tensor("qs_scratch", [2, R, D, B, S], f16, kind="Internal").ap(),
        "e": nc.dram_tensor("e_scratch", [2, H, DH, RW], f16, kind="Internal").ap(),
        "o": nc.dram_tensor("o_scratch", [H + 1, 2 * DH, B, T], f32, kind="Internal").ap(),
        "inv": nc.dram_tensor("inv_scratch", [H + 1, B, T], f32, kind="Internal").ap(),
        "rows": nc.dram_tensor("rows_scratch", [B, 4, D], f32, kind="Internal").ap(),
    }
    from contextlib import ExitStack

    def tools(ctx):
        return (lambda n, sh, dt: ctx.enter_context(nc.sbuf_tensor(n, sh, dt)),
                lambda n, sh, dt: ctx.enter_context(nc.psum_tensor(n, sh, dt)),
                lambda n: ctx.enter_context(nc.semaphore(n)))

    with ExitStack() as whole:
        sb = tools(whole)[0]
        keep = {
            "mods": sb("mods", [P, 6 * KD, B], f32),
            "ident": sb("ident", [P, P], f32),
            "bv": sb("bv", [P, KD], f32),
            "e_shift": [sb(f"e_shift{i}", [P, 2, EW + 1], f16) for i in (0, 1)],
            "e_in": [tools(whole)[2](f"e_in{i}") for i in (0, 1)],
        }
        with ExitStack() as values:
            keep["v_all"] = tools(values)[0]("v_all", [P, B * NT, D], f32)
            for part in (project, attend):
                with ExitStack() as ctx:
                    part(nc, io, scr, keep, *tools(ctx))
        with ExitStack() as ctx:
            ffn(nc, io, scr, keep, *tools(ctx), out)


def kernel(**inputs):
    import ml_dtypes
    import concourse.bacc as bacc
    from concourse.bass_utils import run_bass_kernel_spmd

    a = {k.replace("L0_", "").replace("attn_", "").replace("ffn_", ""): np.asarray(v) for k, v in inputs.items()}
    pos = np.concatenate([np.arange(T - 1, 0, -1, dtype=np.float32), np.arange(0, -T, -1, dtype=np.float32)])
    inv_freq = np.float32(1.0) / np.float32(10000.0) ** (np.float32(2.0) * np.arange(D // 2, dtype=np.float32)
                                                         / np.float32(D))
    angles = pos[:, None] * inv_freq[None, :]
    enc = np.stack([np.sin(angles), np.cos(angles)], axis=-1).reshape(2 * T - 1, D)
    encT = np.zeros((2, D, RW), np.float16)
    encT[0, :, :2 * T - 1] = enc.T
    encT[1, :, :2 * T - 1] = enc.T - encT[0, :, :2 * T - 1].astype(np.float32)
    encT = encT.reshape(2, KD, P, RW).transpose(2, 0, 1, 3)
    mask_b = np.zeros((2, BG, DH, BG, R), np.float16)
    for b in range(BG):
        mask_b[:, b, :, b, :] = 1
    mask_r = np.zeros((R, DH, R), np.float16)
    for r in range(R):
        mask_r[r, :, r] = 1
    spread = np.zeros((NBLK, F), ml_dtypes.bfloat16)
    for n in range(NBLK):
        spread[n, n * F // NBLK:(n + 1) * F // NBLK] = OFF
    arrays = {
        "x": a["x"], "cT": a["c"].T, "wmod": a["wmod"], "ident": np.eye(P, dtype=np.float32),
        "wq": a["Wq"], "wk": a["Wk"], "wv": a["Wv"], "wpos": a["Wpos"], "enc": encT,
        "bq": a["bq"], "bk": a["bk"], "bpos": a["bpos"], "bo": a["bo"], "b2": a["b2"],
        "bv2": a["bv"].reshape(KD, P).T, "wo": a["Wo"], "rwT": a["router_w"].T, "rb": a["router_b"],
        "w1T": a["w1"].T, "b1_2": a["b1"].reshape(FT, P).T, "w2T": a["w2"].T,
        "mask_b": mask_b.reshape(P, BG, R), "mask_r": mask_r.reshape(P, R), "spread": spread,
        "ident_b": np.eye(P, dtype=ml_dtypes.bfloat16),
    }
    arrays = {k: np.ascontiguousarray(v) for k, v in arrays.items()}
    nc = bacc.Bacc("TRN2", target_bir_lowering=False, num_devices=1)
    io = {k: nc.dram_tensor("in_" + k, v.shape, mybir.dt.from_np(v.dtype), kind="ExternalInput").ap()
          for k, v in arrays.items()}
    out = nc.dram_tensor("out_x", (B, T, D), f32, kind="ExternalOutput").ap()
    program(nc, io, out)
    r = run_bass_kernel_spmd(nc, [{"in_" + k: v for k, v in arrays.items()}], core_ids=[0])
    return r.results[0]["out_x"]
```
